# Optimizing a Trainium2 kernel written in Bass

```python
import numpy as np
import jax
import jax.numpy as jnp

def _softmax(x, axis=-1):
    return jax.nn.softmax(x, axis=axis)
def _gelu(x):
    return jax.nn.gelu(x, approximate=True)
def _silu(x):
    return jax.nn.silu(x)
def _sigmoid(x):
    return jax.nn.sigmoid(x)
def _layernorm(x, axis=-1, eps=1e-5):
    m = jnp.mean(x, axis=axis, keepdims=True)
    v = jnp.var(x, axis=axis, keepdims=True)
    return (x - m) / jnp.sqrt(v + eps)
def _scatter_add(tgt, idx, src, axis=0):
    return tgt.at[idx].add(src)
def _segment_sum(src, seg, n):
    return jax.ops.segment_sum(src, seg, n)

kernel_name = 'mk_conv_seq_d2_conv_nchw128_54ff0b'

def setup_inputs(seed: int = 0):
    np.random.seed(seed)
    _w = jnp.asarray
    def _rec_inputs():
        import jax
        import jax.numpy as jnp
        _gk = jax.random.key(seed)
        x = -0.0002928 + 1 * jax.random.normal(jax.random.fold_in(_gk, 1), (8, 128, 64, 64), jnp.float32)
        return x
    x = _rec_inputs()
    def _L0_conv_setup():
        import jax, jax.numpy as jnp
        import numpy as np
        DIM = 128
        HEADS = 8
        K_RATIO = 0.5
        LAYER_SCALE = 0.1
        EPS = 1e-06

        def _group_norm(x, g, b, groups):
            B, C, H, W = x.shape
            xg = x.reshape(B, groups, -1)
            mu = xg.mean(-1, keepdims=True)
            var = xg.var(-1, keepdims=True)
            xn = ((xg - mu) * jax.lax.rsqrt(var + EPS)).reshape(B, C, H, W)
            return xn * g[:, None, None] + b[:, None, None]

        def _conv1x1(x, w):
            return jnp.einsum('oc,bchw->bohw', w, x)

        def _l2norm(t):
            return t / jnp.maximum(jnp.linalg.norm(t, axis=-1, keepdims=True), 1e-12)

        def _sparse_attn(ll, qkv_w, proj_w, g, b):
            B, C, H, W = ll.shape
            N = H * W
            nh = HEADS
            hd = C // nh
            scale = hd ** (-0.5)
            qkv = _conv1x1(ll, qkv_w).reshape(B, 3, nh, hd, N)
            q = jnp.swapaxes(qkv[:, 0], -1, -2)
            k = jnp.swapaxes(qkv[:, 1], -1, -2)
            v = jnp.swapaxes(qkv[:, 2], -1, -2)
            q = _l2norm(q)
            k = _l2norm(k)
            attn = jnp.einsum('bhnd,bhmd->bhnm', q, k) * scale
            attn = jnp.clip(attn, -32.0, 32.0)
            k_num = max(int(N * K_RATIO), 1)
            if k_num < N:
                _, idx = jax.lax.top_k(attn, k_num)
                flat_attn = attn.reshape(-1, N)
                rows = jnp.arange(flat_attn.shape[0])[:, None]
                mask = jnp.zeros(flat_attn.shape, dtype=bool).at[rows, idx.reshape(-1, k_num)].set(True)
                attn = jnp.where(mask.reshape(attn.shape), attn, jnp.float32(-1000000000.0))
            attn = jax.nn.softmax(attn, axis=-1)
            out = jnp.einsum('bhnm,bhmd->bhnd', attn, v)
            out = jnp.swapaxes(out, 2, 3).reshape(B, C, H, W)
            out = _conv1x1(out, proj_w)
            return _group_norm(out, g, b, min(32, C // 4))

        def _high_enhance(h, dw_w, g1, b1, pw_w, g2, b2, alpha):
            C = h.shape[1]
            groups = min(32, C // 8)
            y = jax.lax.conv_general_dilated(h, dw_w, window_strides=(1, 1), padding='SAME', feature_group_count=C, dimension_numbers=('NCHW', 'OIHW', 'NCHW'))
            y = jax.nn.silu(_group_norm(y, g1, b1, groups))
            y = _group_norm(_conv1x1(y, pw_w), g2, b2, groups)
            return h + alpha[0] * y

        def _iwt(ll, lh, hl, hh):
            a = ll - lh - hl + hh
            bq = ll - lh + hl - hh
            c = ll + lh - hl - hh
            d = ll + lh + hl + hh
            B, C, H, W = ll.shape
            row_even = jnp.stack([a, c], axis=-1)
            row_odd = jnp.stack([bq, d], axis=-1)
            h = jnp.stack([row_even, row_odd], axis=3)
            return h.reshape(B, C, 2 * H, 2 * W)

        def _ffn(x, w1, g1, b1, w2, g2, b2):
            d = x.shape[1]
            groups = min(32, d // 4)
            y = _group_norm(_conv1x1(x, w1), g1, b1, groups)
            y = jax.nn.gelu(y, approximate=False)
            return _group_norm(_conv1x1(y, w2), g2, b2, groups)
        key = jax.random.key(seed)
        ks = jax.random.split(key, 18)
        d = DIM
        hd3 = d * 3
        f = lambda k, shape, s=0.05: jax.random.normal(k, shape, dtype=jnp.float32) * s
        return {'x': jax.random.normal(ks[0], (8, d, 64, 64), dtype=jnp.float32), 'qkv_w': f(ks[1], (3 * d, d)), 'proj_w': f(ks[2], (d, d)), 'attn_gn_g': 1.0 + f(ks[3], (d,)), 'attn_gn_b': f(ks[4], (d,)), 'he_dw_w': f(ks[5], (hd3, 1, 3, 3)), 'he_gn1_g': 1.0 + f(ks[6], (hd3,)), 'he_gn1_b': f(ks[7], (hd3,)), 'he_pw_w': f(ks[8], (hd3, hd3)), 'he_gn2_g': 1.0 + f(ks[9], (hd3,)), 'he_gn2_b': f(ks[10], (hd3,)), 'alpha': jnp.array([0.1], dtype=jnp.float32), 'ffn_w1': f(ks[11], (2 * d, d)), 'ffn_gn1_g': 1.0 + f(ks[12], (2 * d,)), 'ffn_gn1_b': f(ks[13], (2 * d,)), 'ffn_w2': f(ks[14], (d, 2 * d)), 'ffn_gn2_g': 1.0 + f(ks[15], (d,)), 'ffn_gn2_b': f(ks[16], (d,))}
    _L0_conv_all = _L0_conv_setup()
    _L0_conv_in = {k: v for k, v in _L0_conv_all.items() if k in ('qkv_w', 'proj_w', 'attn_gn_g', 'attn_gn_b', 'he_dw_w', 'he_gn1_g', 'he_gn1_b', 'he_pw_w', 'he_gn2_g', 'he_gn2_b', 'alpha', 'ffn_w1', 'ffn_gn1_g', 'ffn_gn1_b', 'ffn_w2', 'ffn_gn2_g', 'ffn_gn2_b', )}
    del _L0_conv_all

    def _L1_conv_setup():
        import jax, jax.numpy as jnp
        import numpy as np
        import math
        B, C, H, W = (8, 128, 64, 64)
        R = 16
        key = jax.random.key(seed)
        ks = jax.random.split(key, 10)
        s = 0.05
        return {'x': jax.random.normal(ks[0], (B, C, H, W), dtype=jnp.float32), 'Wq': jax.random.normal(ks[1], (R, C), dtype=jnp.float32) * s, 'bq': jax.random.normal(ks[2], (R,), dtype=jnp.float32) * s, 'Wk': jax.random.normal(ks[3], (R, C), dtype=jnp.float32) * s, 'bk': jax.random.normal(ks[4], (R,), dtype=jnp.float32) * s, 'Wv': jax.random.normal(ks[5], (C, C), dtype=jnp.float32) * s, 'bv': jax.random.normal(ks[6], (C,), dtype=jnp.float32) * s, 'Wo': jax.random.normal(ks[7], (C, C), dtype=jnp.float32) * s, 'bo': jax.random.normal(ks[8], (C,), dtype=jnp.float32) * s, 'gamma': jax.random.normal(ks[9], (1,), dtype=jnp.float32)}
    _L1_conv_all = _L1_conv_setup()
    _L1_conv_in = {k: v for k, v in _L1_conv_all.items() if k in ('Wq', 'bq', 'Wk', 'bk', 'Wv', 'bv', 'Wo', 'bo', 'gamma', )}
    del _L1_conv_all

    return {
        "x": x,
        "L0_conv_qkv_w": _L0_conv_in["qkv_w"],
        "L0_conv_proj_w": _L0_conv_in["proj_w"],
        "L0_conv_attn_gn_g": _L0_conv_in["attn_gn_g"],
        "L0_conv_attn_gn_b": _L0_conv_in["attn_gn_b"],
        "L0_conv_he_dw_w": _L0_conv_in["he_dw_w"],
        "L0_conv_he_gn1_g": _L0_conv_in["he_gn1_g"],
        "L0_conv_he_gn1_b": _L0_conv_in["he_gn1_b"],
        "L0_conv_he_pw_w": _L0_conv_in["he_pw_w"],
        "L0_conv_he_gn2_g": _L0_conv_in["he_gn2_g"],
        "L0_conv_he_gn2_b": _L0_conv_in["he_gn2_b"],
        "L0_conv_alpha": _L0_conv_in["alpha"],
        "L0_conv_ffn_w1": _L0_conv_in["ffn_w1"],
        "L0_conv_ffn_gn1_g": _L0_conv_in["ffn_gn1_g"],
        "L0_conv_ffn_gn1_b": _L0_conv_in["ffn_gn1_b"],
        "L0_conv_ffn_w2": _L0_conv_in["ffn_w2"],
        "L0_conv_ffn_gn2_g": _L0_conv_in["ffn_gn2_g"],
        "L0_conv_ffn_gn2_b": _L0_conv_in["ffn_gn2_b"],
        "L1_conv_Wq": _L1_conv_in["Wq"],
        "L1_conv_bq": _L1_conv_in["bq"],
        "L1_conv_Wk": _L1_conv_in["Wk"],
        "L1_conv_bk": _L1_conv_in["bk"],
        "L1_conv_Wv": _L1_conv_in["Wv"],
        "L1_conv_bv": _L1_conv_in["bv"],
        "L1_conv_Wo": _L1_conv_in["Wo"],
        "L1_conv_bo": _L1_conv_in["bo"],
        "L1_conv_gamma": _L1_conv_in["gamma"],
    }

def reference(x, L0_conv_qkv_w, L0_conv_proj_w, L0_conv_attn_gn_g, L0_conv_attn_gn_b, L0_conv_he_dw_w, L0_conv_he_gn1_g, L0_conv_he_gn1_b, L0_conv_he_pw_w, L0_conv_he_gn2_g, L0_conv_he_gn2_b, L0_conv_alpha, L0_conv_ffn_w1, L0_conv_ffn_gn1_g, L0_conv_ffn_gn1_b, L0_conv_ffn_w2, L0_conv_ffn_gn2_g, L0_conv_ffn_gn2_b, L1_conv_Wq, L1_conv_bq, L1_conv_Wk, L1_conv_bk, L1_conv_Wv, L1_conv_bv, L1_conv_Wo, L1_conv_bo, L1_conv_gamma):
    import jax
    import jax.numpy as jnp
    def _L0_conv_ref(x, qkv_w, proj_w, attn_gn_g, attn_gn_b, he_dw_w, he_gn1_g, he_gn1_b, he_pw_w, he_gn2_g, he_gn2_b, alpha, ffn_w1, ffn_gn1_g, ffn_gn1_b, ffn_w2, ffn_gn2_g, ffn_gn2_b):
        import jax, jax.numpy as jnp
        import numpy as np
        DIM = 128
        HEADS = 8
        K_RATIO = 0.5
        LAYER_SCALE = 0.1
        EPS = 1e-06

        def _group_norm(x, g, b, groups):
            B, C, H, W = x.shape
            xg = x.reshape(B, groups, -1)
            mu = xg.mean(-1, keepdims=True)
            var = xg.var(-1, keepdims=True)
            xn = ((xg - mu) * jax.lax.rsqrt(var + EPS)).reshape(B, C, H, W)
            return xn * g[:, None, None] + b[:, None, None]

        def _conv1x1(x, w):
            return jnp.einsum('oc,bchw->bohw', w, x)

        def _l2norm(t):
            return t / jnp.maximum(jnp.linalg.norm(t, axis=-1, keepdims=True), 1e-12)

        def _sparse_attn(ll, qkv_w, proj_w, g, b):
            B, C, H, W = ll.shape
            N = H * W
            nh = HEADS
            hd = C // nh
            scale = hd ** (-0.5)
            qkv = _conv1x1(ll, qkv_w).reshape(B, 3, nh, hd, N)
            q = jnp.swapaxes(qkv[:, 0], -1, -2)
            k = jnp.swapaxes(qkv[:, 1], -1, -2)
            v = jnp.swapaxes(qkv[:, 2], -1, -2)
            q = _l2norm(q)
            k = _l2norm(k)
            attn = jnp.einsum('bhnd,bhmd->bhnm', q, k) * scale
            attn = jnp.clip(attn, -32.0, 32.0)
            k_num = max(int(N * K_RATIO), 1)
            if k_num < N:
                _, idx = jax.lax.top_k(attn, k_num)
                flat_attn = attn.reshape(-1, N)
                rows = jnp.arange(flat_attn.shape[0])[:, None]
                mask = jnp.zeros(flat_attn.shape, dtype=bool).at[rows, idx.reshape(-1, k_num)].set(True)
                attn = jnp.where(mask.reshape(attn.shape), attn, jnp.float32(-1000000000.0))
            attn = jax.nn.softmax(attn, axis=-1)
            out = jnp.einsum('bhnm,bhmd->bhnd', attn, v)
            out = jnp.swapaxes(out, 2, 3).reshape(B, C, H, W)
            out = _conv1x1(out, proj_w)
            return _group_norm(out, g, b, min(32, C // 4))

        def _high_enhance(h, dw_w, g1, b1, pw_w, g2, b2, alpha):
            C = h.shape[1]
            groups = min(32, C // 8)
            y = jax.lax.conv_general_dilated(h, dw_w, window_strides=(1, 1), padding='SAME', feature_group_count=C, dimension_numbers=('NCHW', 'OIHW', 'NCHW'))
            y = jax.nn.silu(_group_norm(y, g1, b1, groups))
            y = _group_norm(_conv1x1(y, pw_w), g2, b2, groups)
            return h + alpha[0] * y

        def _iwt(ll, lh, hl, hh):
            a = ll - lh - hl + hh
            bq = ll - lh + hl - hh
            c = ll + lh - hl - hh
            d = ll + lh + hl + hh
            B, C, H, W = ll.shape
            row_even = jnp.stack([a, c], axis=-1)
            row_odd = jnp.stack([bq, d], axis=-1)
            h = jnp.stack([row_even, row_odd], axis=3)
            return h.reshape(B, C, 2 * H, 2 * W)

        def _ffn(x, w1, g1, b1, w2, g2, b2):
            d = x.shape[1]
            groups = min(32, d // 4)
            y = _group_norm(_conv1x1(x, w1), g1, b1, groups)
            y = jax.nn.gelu(y, approximate=False)
            return _group_norm(_conv1x1(y, w2), g2, b2, groups)
        x1 = x[:, :, 0::2, 0::2]
        x2 = x[:, :, 1::2, 0::2]
        x3 = x[:, :, 0::2, 1::2]
        x4 = x[:, :, 1::2, 1::2]
        ll = (x1 + x2 + x3 + x4) * 0.5
        lh = (-x1 - x2 + x3 + x4) * 0.5
        hl = (-x1 + x2 - x3 + x4) * 0.5
        hh = (x1 - x2 - x3 + x4) * 0.5
        high = jnp.concatenate([lh, hl, hh], axis=1)
        ll_out = _sparse_attn(ll, qkv_w, proj_w, attn_gn_g, attn_gn_b)
        high_out = _high_enhance(high, he_dw_w, he_gn1_g, he_gn1_b, he_pw_w, he_gn2_g, he_gn2_b, alpha)
        C = ll.shape[1]
        x_rec = _iwt(ll + ll_out, high_out[:, :C], high_out[:, C:2 * C], high_out[:, 2 * C:])
        out = x + LAYER_SCALE * x_rec
        out = out + LAYER_SCALE * _ffn(out, ffn_w1, ffn_gn1_g, ffn_gn1_b, ffn_w2, ffn_gn2_g, ffn_gn2_b)
        return out

    def _L1_conv_ref(x, Wq, bq, Wk, bk, Wv, bv, Wo, bo, gamma):
        import jax, jax.numpy as jnp
        import numpy as np
        import math
        B, C, H, W = (8, 128, 64, 64)
        R = 16
        b, c, h, w = x.shape
        n = h * w
        xf = x.reshape(b, c, n)
        q = jnp.einsum('rc,bcn->bnr', Wq, xf) + bq
        k = jnp.einsum('rc,bcn->brn', Wk, xf) + bk[:, None]
        v = jnp.einsum('oc,bcn->bon', Wv, xf) + bv[:, None]
        scale = 1.0 / math.sqrt(R)
        attn = jax.nn.softmax(jnp.einsum('bnr,brm->bnm', q, k) * scale, axis=-1)
        out = jnp.einsum('bcm,bnm->bcn', v, attn)
        out = jnp.einsum('oc,bcn->bon', Wo, out) + bo[:, None]
        out = gamma[0] * out + xf
        return out.reshape(b, c, h, w)

    def _gn(v, G=32, eps=1e-5):
        B_, C_, H_, W_ = v.shape
        g = v.reshape(B_, G, C_ // G, H_, W_)
        m = jnp.mean(g, axis=(2, 3, 4), keepdims=True)
        s = jnp.var(g, axis=(2, 3, 4), keepdims=True)
        return ((g - m) / jnp.sqrt(s + eps)).reshape(v.shape)

    def _ln_c(v, eps=1e-6):
        m = jnp.mean(v, axis=1, keepdims=True)
        s = jnp.var(v, axis=1, keepdims=True)
        return (v - m) / jnp.sqrt(s + eps)

    def _ln_t(v, eps=1e-5):
        m = jnp.mean(v, axis=-1, keepdims=True)
        s = jnp.var(v, axis=-1, keepdims=True)
        return (v - m) / jnp.sqrt(s + eps)

    def _to_tokens(v):
        B_, C_, H_, W_ = v.shape
        return v.reshape(B_, C_, H_ * W_).transpose(0, 2, 1)
    def _from_tokens(t, like):
        B_, C_, H_, W_ = like.shape
        return t.transpose(0, 2, 1).reshape(B_, C_, H_, W_)

    x = _L0_conv_ref(x, L0_conv_qkv_w, L0_conv_proj_w, L0_conv_attn_gn_g, L0_conv_attn_gn_b, L0_conv_he_dw_w, L0_conv_he_gn1_g, L0_conv_he_gn1_b, L0_conv_he_pw_w, L0_conv_he_gn2_g, L0_conv_he_gn2_b, L0_conv_alpha, L0_conv_ffn_w1, L0_conv_ffn_gn1_g, L0_conv_ffn_gn1_b, L0_conv_ffn_w2, L0_conv_ffn_gn2_g, L0_conv_ffn_gn2_b)
    x = _L1_conv_ref(x, L1_conv_Wq, L1_conv_bq, L1_conv_Wk, L1_conv_bk, L1_conv_Wv, L1_conv_bv, L1_conv_Wo, L1_conv_bo, L1_conv_gamma)
    return x


_drawn_inputs = setup_inputs


def setup_inputs(seed=0):
    import zlib

    import numpy as np

    out = dict(_drawn_inputs(seed))
    spreads = {}
    factors = {'L0_conv_attn_gn_g': 8.0,
     'L0_conv_attn_gn_b': 8.0,
     'L0_conv_he_dw_w': 4.254,
     'L0_conv_he_gn1_g': 8.0,
     'L0_conv_he_gn1_b': 8.0,
     'L0_conv_he_pw_w': 3.919,
     'L0_conv_he_gn2_g': 8.0,
     'L0_conv_he_gn2_b': 8.0,
     'L0_conv_ffn_gn1_g': 8.0,
     'L0_conv_ffn_gn1_b': 8.0,
     'L0_conv_ffn_gn2_g': 8.0,
     'L0_conv_ffn_gn2_b': 8.0,
     'L1_conv_Wq': 8.0,
     'L1_conv_bq': 8.0,
     'L1_conv_Wk': 8.0,
     'L1_conv_bk': 64.0,
     'L1_conv_Wv': 8.0,
     'L1_conv_bv': 8.0,
     'L1_conv_Wo': 8.0,
     'L1_conv_bo': 45.222}
    for name, (base, spread) in spreads.items():
        noise = np.random.default_rng([zlib.crc32(name.encode()), seed]).standard_normal(out[name].shape)
        drawn = base * np.exp(spread * noise) if base else spread * noise
        out[name] = jnp.asarray(drawn.astype(out[name].dtype))
    for name, factor in factors.items():
        out[name] = (out[name] * factor).astype(out[name].dtype)
    return out
```

```python
import concourse.bass as bass
from concourse import mybir
from contextlib import ExitStack
import numpy as np

B, C, H, W = 8, 128, 64, 64
N1 = H * W
HH = H // 2
N0 = HH * HH
NH, HD = 8, 16
KEEP = N0 // 2
NT = N0 // 128
PAIRS = NH // 2
R = 16
MT1 = N1 // 128
NCH = N1 // 512
TERMS = [(0, 0), (0, 1), (1, 0), (1, 1), (0, 2), (2, 0)]
KS = 16 * len(TERMS)
KA = KS + 3
COUNTS = 6
NA = 5
BISECT = 32
AIM = KEEP - 4
SLOPE = 6266.0
HALF = 0.02

V_AG, V_AB, V_H1G, V_H1B, V_H2G, V_H2B, V_F1G, V_F1B, V_F2G, V_F2B = 0, 1, 2, 5, 8, 11, 14, 16, 18, 19
V_BQK, V_BV, V_BO, V_ALPHA, V_GAMMA, NVEC = 20, 21, 22, 23, 24, 25
GN_CH = [4, 12, 12, 8, 4]
GN_BLK = [1, 3, 3, 2, 1]
GN_G = [V_AG, V_H1G, V_H2G, V_F1G, V_F2G]
GN_B = [V_AB, V_H1B, V_H2B, V_F1B, V_F2B]
GN_IND = [0, 1, 1, 4, 0]


class Chain:

    def __init__(self, eng, sem):
        self.eng, self.sem, self.n = eng, sem, 0
        eng.sem_clear(sem)

    def did(self, ins):
        self.n += 1
        ins.then_inc(self.sem, 1)
        return ins

    def wait(self):
        self.eng.wait_ge(self.sem, self.n)

    def link(self, ins):
        self.did(ins)
        self.wait()


def dwt_attention_kernel(nc, x, qkvT, projT, dw, pwT, w1T, w2T, qk1T, wv, woT, vec, cst, cstT, out,
                         images=B, taps=None):
    fp32, bf16, u32 = mybir.dt.float32, mybir.dt.bfloat16, mybir.dt.uint32
    ALU, ACT, AX = mybir.AluOpType, mybir.ActivationFunctionType, mybir.AxisListType
    ctx = ExitStack()
    with ctx:
        def sb(name, shape, dt=fp32):
            return ctx.enter_context(nc.sbuf_tensor(name, shape, dt))

        def sem(name):
            return ctx.enter_context(nc.semaphore(name))

        scr0 = nc.dram_tensor("scr0", [3, 2, 128, N0], bf16, kind="Internal").ap()
        scr1 = nc.dram_tensor("scr1", [3, 128, N0], bf16, kind="Internal").ap()

        w_qkv = sb("w_qkv", [128, 384])
        w_proj = sb("w_proj", [128, 128])
        w_dw = sb("w_dw", [128, 27])
        w_pw = sb("w_pw", [128, 3, 384])
        w_1 = sb("w_1", [128, 256])
        w_2 = sb("w_2", [128, 2, 128])
        w_qk1 = sb("w_qk1", [128, 32])
        w_v = sb("w_v", [128, 128])
        w_oT = sb("w_oT", [128, 128])
        w_vo = sb("w_vo", [128, 128])
        vecs = sb("vecs", [128, NVEC])
        gbo = sb("gbo", [128, 1])
        cons = sb("cons", [128, 128 + 8 + 7 + 6 * 32])
        ident = cons[:, 0:128]
        headind = cons[:, 128:136]
        window = cons[:, 136:143]
        inds = cons[:, 143:].rearrange("p (k g) -> p k g", g=32)
        indT = sb("indT", [32, 6, 128])
        identb = sb("identb", [128, 128], bf16)
        mhalf = sb("mhalf", [128, 128])
        diag = sb("diag", [128, 27, 128])
        Xin = sb("Xin", [128, N1])
        X1 = sb("X1", [128, N1])
        arena = sb("arena", [128, 2 * NT, N0])
        QPKP = sb("QPKP", [128, 2, NH, N0], bf16)
        QP, KP = QPKP[:, 0], QPKP[:, 1]
        LL = sb("LL", [128, N0])
        PAD = sb("PAD", [128, 3, HH + 2, HH + 2])
        VT = sb("VT", [128, NT, NH, HD + 1])
        O = sb("O", [128, NT, NH, HD])
        JA = sb("JA", [128, 2, N0])
        JD = sb("JD", [128, 2, N0])
        SUM = sb("SUM", [128, 2, NT])
        CA = sb("CA", [128, 2, NT])
        CD = sb("CD", [128, 2, NT])
        TE = sb("TE", [128, 2, 2, NT])
        BR = sb("BR", [128, 2, 2, 2, NT])
        MK = sb("MK", [128, 2, 2, NT], u32)
        MK2 = sb("MK2", [128, 2, NT], u32)
        E2 = sb("E2", [128, 2, NT])
        DD = sb("DD", [128, 2, 2, NT])
        DR = sb("DR", [128, 2, NT])
        TN = sb("TN", [128, 2, NT])
        M8 = sb("M8", [128, 2, NT, 8])
        OH = sb("OH", [128, 2, NT, 7])
        PM = sb("PM", [128, 2, NT, 7])
        TS = sb("TS", [128, 2, NT])
        TR = sb("TR", [128, 2, NT])
        TP = sb("TP", [128, 2, 3, NT], bf16)
        TPT = sb("TPT", [24, 2, 128], bf16)
        FOUND = sb("FOUND", [128, 2, 1])
        FOUNDI = sb("FOUNDI", [1, 1], mybir.dt.int32)
        RO = sb("RO", [128, NT])
        SSM = sb("SSM", [128, 128])
        RN = sb("RN", [128, 128])
        BN = sb("BN", [128, 16, 6])
        MV = sb("MV", [128, 3, 2])
        ST = sb("ST", [128, 3, 2])
        GG = sb("GG", [32, 2])
        GV = sb("GV", [32, 2])
        SC = sb("SC", [128, 3])
        SH = sb("SH", [128, 3])
        SM = sb("SM", [128, 3])
        MX = sb("MX", [128, 4, NCH])
        MM = sb("MM", [128, 4])
        MR = sb("MR", [128, 4])
        MP = sb("MP", [128, 3, 4], bf16)
        MPT = sb("MPT", [12, 128], bf16)
        RD = sb("RD", [128, 4])
        JAb = JA[:, :, :].rearrange("p a n -> p (a n)").bitcast(bf16).rearrange("p (a n) -> p a n", n=N0)
        JDb = JD[:, :, :].rearrange("p a n -> p (a n)").bitcast(bf16).rearrange("p (a n) -> p a n", n=N0)
        flat = arena[:, :, :].rearrange("p a n -> p (a n)")
        DW = flat[:, 0:4 * N0].rearrange("p (k n) -> p k n", k=4)
        UU = flat[:, 4 * N0:8 * N0].rearrange("p (k n) -> p k n", k=4)
        SQ = flat[:, 8 * N0:10 * N0]
        QK = flat[:, 10 * N0:12 * N0]
        PT = flat[:, 12 * N0:15 * N0].bitcast(bf16).rearrange("p (a n) -> p a n", a=3)
        RE = flat[:, 0:2 * N0].rearrange("p (k c) -> p k c", c=128)
        OC = flat[:, 0:N0]
        Y = flat[:, N0:4 * N0].rearrange("p (k n) -> p k n", k=3)
        DL = flat[:, 4 * N0:8 * N0].rearrange("p (k n) -> p k n", k=4)
        IW = flat[:, 8 * N0:12 * N0].rearrange("p (k n) -> p k n", k=4)
        IX = flat[:, 12 * N0:16 * N0].rearrange("p (k n) -> p k n", k=4)
        HF = flat[:, 0:8 * N0].rearrange("p (o n) -> p o n", o=2)
        F2 = flat[:, 8 * N0:12 * N0]
        Q1 = flat[:, 12 * N0:13 * N0]
        PT1 = flat[:, 13 * N0:15 * N0].bitcast(bf16)[:, 0:3 * N0].rearrange("p (a n) -> p a n", a=3)
        V1 = flat[:, 0:MT1 * 129].rearrange("p (m c) -> p m c", c=129)
        P1 = flat[:, 5 * N0:7 * N0].rearrange("p (k n) -> p k n", n=512)
        ON = flat[:, 7 * N0:7 * N0 + 512].rearrange("p (i c) -> p i c", c=128)
        YO = flat[:, 8 * N0:9 * N0].rearrange("p (k n) -> p k n", n=512)
        QP1 = QPKP[:, 0].rearrange("p h n -> p (h n)")[:, 0:N1]
        KP1 = QPKP[:, 1].rearrange("p h n -> p (h n)")[:, 0:N1]

        PS = ctx.enter_context(nc.psum_tensor("PS", [128, 8, 512], fp32))

        def bank2(k):
            return PS[:, 2 * k:2 * k + 2, :].rearrange("p a n -> p (a n)")

        NWT = 13
        names = """w ws wvo cst xin dwt ll pad qk sq qkc ss ssm re rb qkn p0 r1 p1 p2 scrw qp v vt
          S eva evd t ca cd tp tt tpt qt st e p pv o apair dpair ot oc pj fnd fsum g1 g2 g3 g4 g5 dll cv y pw dl iw x1 xfree
          f1 hc ge f2 f2c f2n x2 q1 q1c p10 r11 p11 p12 scrw1 qp1 v1p v1c m mr mp mt mpt mq st1 e1 pv1 pvd on nt y1 out
          enda endd dset dimg dpr dch dgn pimg poolset""".split()
        s = {n: sem("s_" + n) for n in names}
        block = ctx.enter_context(nc.Block())

        @block.sync
        def _(sp):
            for dst, src in ((w_qkv, qkvT), (w_proj, projT), (w_dw, dw), (w_pw, pwT), (w_1, w1T), (w_2, w2T),
                             (w_qk1, qk1T), (w_v, wv), (w_oT, woT), (vecs, vec), (cons, cst), (indT, cstT)):
                sp.dma_start(dst[:], src).then_inc(s["w"], 16)
            with sp.Fori(0, images) as b:
                sp.wait_ge(s["xfree"], b + 1)
                sp.dma_start(Xin[:, :], x[bass.ds(b, 1)].rearrange("a c n -> c (a n)")).then_inc(s["xin"], 16)
                sp.wait_ge(s["p2"], b + 1)
                for a in range(3):
                    sp.dma_start(scr0[a].rearrange("q p n -> p q n"),
                                 PT[:, a, :].rearrange("p (q n) -> p q n", q=2)).then_inc(s["scrw"], 16)
                sp.wait_ge(s["scrw"], (b + 1) * 48)
                for j, (tq, tk) in enumerate(TERMS):
                    for w, (t, dst) in enumerate(((tq, QP), (tk, KP))):
                        sp.dma_start(dst[16 * j:16 * j + 16], scr0[t, w].rearrange("(h d) n -> d h n", d=HD))\
                            .then_inc(s["qp"], 16)
                with sp.Fori(0, PAIRS) as pr:
                    for hh in range(2):
                        sp.wait_ge(s["tpt"], (b * PAIRS + pr) * 2 + hh + 1)
                        for a in range(3):
                            sp.dma_start(QP[KS + a:KS + a + 1, bass.ds(pr * 2 + hh, 1), :].rearrange("p h (i n) -> p (h i) n", n=128),
                                         TPT[8 * a:8 * a + 8, hh, :]).then_inc(s["qt"], 16)
                sp.wait_ge(s["p12"], b + 1)
                for a in range(3):
                    sp.dma_start(scr1[a], PT1[:, a, :]).then_inc(s["scrw1"], 16)
                sp.wait_ge(s["scrw1"], (b + 1) * 48)
                for j, (tq, tk) in enumerate(TERMS):
                    for w, (t, dst) in enumerate(((tq, QP1), (tk, KP1))):
                        sp.dma_start(dst[16 * j:16 * j + 16].rearrange("p (j n) -> p j n", j=4),
                                     scr1[t].rearrange("(j s) n -> s j n", s=32)[16 * w:16 * w + 16]).then_inc(s["qp1"], 16)
                def max_rows(j, k):
                    sp.wait_ge(s["mpt"], k)
                    for a in range(3):
                        sp.dma_start(QP1[KS + a:KS + a + 1, bass.ds(j * 512, 512)].rearrange("p (i n) -> p i n", n=128),
                                     MPT[4 * a:4 * a + 4, :]).then_inc(s["mq"], 16)

                def store(j, k):
                    sp.wait_ge(s["y1"], k)
                    sp.dma_start(out[bass.ds(b, 1), :, bass.ds(j * 512, 512)].rearrange("a c n -> c (a n)"),
                                 YO[:, 0, :]).then_inc(s["out"], 16)

                max_rows(0, b * NCH + 1)
                with sp.Fori(0, NCH - 1) as j:
                    max_rows(j + 1, b * NCH + j + 2)
                    store(j, b * NCH + j + 1)
                store(NCH - 1, b * NCH + NCH)
            sp.wait_ge(s["out"], (images * NCH + 1) * 16)

        @block.tensor
        def _(pe):
            mm = nc.tensor.matmul

            def gn(b, g, n):
                pe.wait_ge(s["g1"], b * 5 + g + 1)
                for k in range(n):
                    last = mm(PS[0:32, 7, 0:2], inds[:, GN_IND[g] + k, :], ST[:, k, :], start=(k == 0), stop=(k == n - 1))
                last.then_inc(s["g2"], 1)
                pe.wait_ge(s["g4"], b * 5 + g + 1)
                for k in range(n):
                    last = mm(PS[:, 7, 8 + 2 * k:10 + 2 * k], indT[:, GN_IND[g] + k, :], GG[:, :], start=True, stop=True)
                last.then_inc(s["g5"], 1)

            pe.wait_ge(s["w"], 16 * 12)
            mm(PS[:, 0, 0:128], w_v[:, :], w_oT[:, :], start=True, stop=True)
            mm(PS[:, 1, 0:1], w_oT[:, :], vecs[:, V_BV:V_BV + 1], start=True, stop=True).then_inc(s["wvo"], 1)
            pe.wait_ge(s["dset"], DSET)
            with pe.Fori(0, images) as b:
                pe.wait_ge(s["endd"], b + 1)
                pe.wait_ge(s["enda"], b + 1)
                pe.wait_ge(s["ll"], b + 1)
                for g in range(2):
                    for h in range(2):
                        last = mm(PS[:, 2 * g + h, :], w_qkv[:, 128 * g:128 * g + 128], LL[:, 512 * h:512 * h + 512],
                                  start=True, stop=True)
                last.then_inc(s["qk"], 1)
                pe.wait_ge(s["sq"], b + 1)
                for nt in range(NT):
                    for g in range(2):
                        k = nt * 2 + g
                        last = mm(PS[:, 4, 8 * k:8 * k + 8], SQ[:, g * N0 + nt * 128:g * N0 + nt * 128 + 128], headind,
                                  start=True, stop=True)
                last.then_inc(s["ss"], 1)
                pe.wait_ge(s["qkc"], b + 1)
                for mt in range(NT):
                    last = mm(PS[:, mt // 4, (mt % 4) * 128:(mt % 4) * 128 + 128], LL[:, mt * 128:mt * 128 + 128],
                              w_qkv[:, 256:384], start=True, stop=True)
                last.then_inc(s["v"], 1)
                pe.wait_ge(s["re"], b + 1)
                for g in range(2):
                    for nt in range(NT):
                        last = mm(PS[:, 4 + 2 * g + nt // 4, (nt % 4) * 128:(nt % 4) * 128 + 128], RE[:, nt * 2 + g, :],
                                  ident, start=True, stop=True)
                last.then_inc(s["rb"], 1)
                with pe.Fori(0, PAIRS) as pr:
                    P = b * PAIRS + pr
                    pe.wait_ge(s["qp"], (b + 1) * 192)
                    pe.wait_ge(s["vt"], b + 1)
                    pe.wait_ge(s["apair"], P + 1)
                    pe.wait_ge(s["dpair"], P + 1)
                    for tl in range(2 * NT):
                        hh, i = divmod(tl, NT)
                        if tl >= 4:
                            pe.wait_ge(s["eva" if tl % 2 == 0 else "evd"], P * NT + (tl - 4) // 2 + 1)
                        for h in range(2):
                            last = mm(PS[:, 2 * (tl % 4) + h, :], QP[0:KS, bass.ds(pr * 2 + hh, 1), 128 * i:128 * i + 128],
                                      KP[0:KS, bass.ds(pr * 2 + hh, 1), 512 * h:512 * h + 512], start=True, stop=True)
                        last.then_inc(s["S"], 1)
                    for hh in range(2):
                        pe.wait_ge(s["fnd"], P * 2 + hh + 1)
                        mm(PS[0:1, 7, 256:257], FOUND[:, hh, :], mhalf[:, 0:1], start=True, stop=True).then_inc(s["fsum"], 1)
                        pe.wait_ge(s["tp"], P * 2 + hh + 1)
                        mm(PS[0:24, 7, 0:128], TP[:, hh].rearrange("p a i -> p (a i)"), identb[:, :],
                           start=True, stop=True).then_inc(s["tt"], 1)
                        pe.wait_ge(s["qt"], (P * 2 + hh + 1) * 48)
                        for mt in range(NT):
                            if hh * NT + mt >= 2:
                                pe.wait_ge(s["p"], P * 2 * NT + hh * NT + mt - 1)
                            for h in range(2):
                                last = mm(PS[:, 2 * (mt % 2) + h, :], KP[0:KA, bass.ds(pr * 2 + hh, 1), 128 * mt:128 * mt + 128],
                                          QP[0:KA, bass.ds(pr * 2 + hh, 1), 512 * h:512 * h + 512], start=True, stop=True)
                            last.then_inc(s["st"], 1)
                        pe.wait_ge(s["p"], P * 2 * NT + hh * NT + NT)
                        if hh == 1:
                            pe.wait_ge(s["o"], P * 2 + 1)
                        for i in range(NT):
                            for mt in range(NT):
                                last = mm(PS[:, 6, 17 * i:17 * i + 17], arena[:, hh * NT + mt, 128 * i:128 * i + 128],
                                          VT[:, mt, bass.ds(pr * 2 + hh, 1), :], start=(mt == 0), stop=(mt == NT - 1))
                        last.then_inc(s["pv"], 1)
                pe.wait_ge(s["o"], (b + 1) * NH)
                for i in range(NT):
                    last = mm(PS[:, i // 4, (i % 4) * 128:(i % 4) * 128 + 128], O[:, i].rearrange("p h d -> p (h d)"), ident,
                              start=True, stop=True)
                last.then_inc(s["ot"], 1)
                pe.wait_ge(s["oc"], b + 1)
                for h in range(2):
                    last = mm(PS[:, 2 + h, :], w_proj[:, :], OC[:, 512 * h:512 * h + 512], start=True, stop=True)
                last.then_inc(s["pj"], 1)
                gn(b, 0, 1)
                pe.wait_ge(s["pad"], (b + 1) * 3)
                pe.wait_ge(s["dll"], b + 1)
                for k in range(3):
                    for h in range(2):
                        for t in range(9):
                            last = mm(PS[:, 2 * k + h, :].rearrange("p (y x) -> p y x", x=HH), diag[:, 9 * k + t, :],
                                      PAD[:, k, 16 * h + t // 3:16 * h + t // 3 + 16, t % 3:t % 3 + HH],
                                      start=(t == 0), stop=(t == 8))
                    last.then_inc(s["cv"], 1)
                gn(b, 1, 3)
                pe.wait_ge(s["y"], (b + 1) * 3)
                for o in range(3):
                    for h in range(2):
                        for k in range(3):
                            last = mm(PS[:, 2 * o + h, :], w_pw[:, k, 128 * o:128 * o + 128], Y[:, k, 512 * h:512 * h + 512],
                                      start=(k == 0), stop=(k == 2))
                    last.then_inc(s["pw"], 1)
                gn(b, 2, 3)
                pe.wait_ge(s["x1"], (b + 1) * 4)
                pe.wait_ge(s["dl"], (b + 1) * 3)
                for k in range(16):
                    o, ch = divmod(k, 8)
                    if k >= 6:
                        pe.wait_ge(s["hc"], b * 16 + k - 5)
                    mm(PS[:, k % 6, :], w_1[:, 128 * o:128 * o + 128], X1[:, 512 * ch:512 * ch + 512],
                       start=True, stop=True).then_inc(s["f1"], 1)
                gn(b, 3, 2)
                for ch in range(8):
                    pe.wait_ge(s["ge"], b * 8 + 2 * (ch // 2) + 2)
                    if ch >= 6:
                        pe.wait_ge(s["f2c"], b * 8 + ch - 5)
                    for o in range(2):
                        last = mm(PS[:, ch % 6, :], w_2[:, o, :], HF[:, o, 512 * ch:512 * ch + 512], start=(o == 0), stop=(o == 1))
                    last.then_inc(s["f2"], 1)
                gn(b, 4, 1)
                pe.wait_ge(s["x2"], (b + 1) * 4)
                for j in range(4):
                    for h in range(2):
                        last = mm(PS[32 * j:32 * j + 32, h, :], w_qk1[:, :], X1[:, j * N0 + 512 * h:j * N0 + 512 * h + 512],
                                  start=True, stop=True, tile_position=(0, 32 * j))
                last.then_inc(s["q1"], 1)
                for k in range(8):
                    if k >= 4:
                        pe.wait_ge(s["v1c"], b * 8 + k - 3)
                    for m in range(4):
                        mt = 4 * k + m
                        last = mm(PS[:, 2 + k % 4, 128 * m:128 * m + 128], X1[:, 128 * mt:128 * mt + 128], w_vo[:, :],
                                  start=True, stop=True)
                    last.then_inc(s["v1p"], 1)
                pe.wait_ge(s["qp1"], (b + 1) * 192)
                pe.wait_ge(s["q1c"], b + 1)
                pe.wait_ge(s["v1c"], (b + 1) * 8)

                def maxima(j, k, base):
                    i, ch = divmod(k, NCH)
                    if k >= 3 or not isinstance(j, int):
                        pe.wait_ge(s["mr"], base + max(k - 2, 0))
                    mm(PS[:, k % 3, :], QP1[0:KS, bass.ds(j * 512 + 128 * i, 128)], KP1[0:KS, 512 * ch:512 * ch + 512],
                       start=True, stop=True).then_inc(s["m"], 1)

                def maxrow(k):
                    pe.wait_ge(s["mp"], k)
                    mm(PS[0:12, 3, 0:128], MP[:, :, :].rearrange("p a i -> p (a i)"), identb[:, :],
                       start=True, stop=True).then_inc(s["mt"], 1)

                def turn(k):
                    pe.wait_ge(s["on"], k)
                    for i in range(4):
                        last = mm(PS[:, 3, 128 * i:128 * i + 128], ON[:, i, :], ident, start=True, stop=True)
                    last.then_inc(s["nt"], 1)

                def chunk(j, more):
                    J = b * NCH + j
                    pe.wait_ge(s["mq"], (J + 1) * 48)
                    done = 0
                    for mt in range(MT1 + 1):
                        if mt < MT1:
                            if mt >= 2:
                                pe.wait_ge(s["e1"], J * MT1 + mt - 1)
                            mm(PS[:, 4 + mt % 2, :], KP1[0:KA, 128 * mt:128 * mt + 128], QP1[0:KA, bass.ds(j * 512, 512)],
                               start=True, stop=True).then_inc(s["st1"], 1)
                            if more:
                                while done < min(32, (mt + 1) * 4 // 3):
                                    maxima(j + 1, done, (J + 1) * 32)
                                    done += 1
                            if more and mt == 28:
                                maxrow(J + 2)
                        if mt >= 1:
                            m = mt - 1
                            pe.wait_ge(s["e1"], J * MT1 + m + 1)
                            if m == 0:
                                pe.wait_ge(s["on"], J + 1)
                            for i in range(4):
                                last = mm(PS[:, 6 + i // 2, 136 * (i % 2):136 * (i % 2) + 129], P1[:, m % 4, 128 * i:128 * i + 128],
                                          V1[:, m, :], start=(m == 0 and i % 2 == 0), stop=(m == MT1 - 1),
                                          skip_group_check=True)
                            last.then_inc(s["pv1"], 1)
                    if more:
                        pe.wait_ge(s["mpt"], J + 2)
                    turn(J + 2)

                for k in range(32):
                    maxima(0, k, b * NCH * 32)
                maxrow(b * NCH + 1)
                with pe.Fori(0, NCH - 1) as j:
                    chunk(j, True)
                chunk(NCH - 1, False)

        @block.scalar
        def _(act):
            A = nc.scalar.activation
            act.wait_ge(s["wvo"], 1)
            A(w_vo[:, :], PS[:, 0, 0:128], ACT.Copy).then_inc(s["ws"], 1)
            act.wait_ge(s["dset"], DSET)
            act.sem_inc(s["enda"], 1)
            act.sem_inc(s["apair"], 1)
            with act.Fori(0, images) as b:
                for k in range(4):
                    act.wait_ge(s["dwt"], b * 4 + k + 1)
                    if k == 0:
                        A(LL[:, :], UU[:, 0, :], ACT.Copy, scale=0.5).then_inc(s["ll"], 1)
                    else:
                        A(PAD[:, k - 1, 1:HH + 1, 1:HH + 1], UU[:, k, :].rearrange("p (y x) -> p y x", x=HH), ACT.Copy,
                          scale=0.5).then_inc(s["pad"], 1)
                act.wait_ge(s["qk"], b + 1)
                qk_ps = PS[:, 0:4, :].rearrange("p a n -> p (a n)")
                A(SQ, qk_ps, ACT.Square).then_inc(s["sq"], 1)
                A(QK, qk_ps, ACT.Copy).then_inc(s["qkc"], 1)
                act.wait_ge(s["v"], b + 1)
                for h in range(2):
                    last = A(VT[:, 4 * h:4 * h + 4, :, 0:HD], PS[:, h, :].rearrange("p (m h d) -> p m h d", h=NH, d=HD), ACT.Copy)
                last.then_inc(s["vt"], 1)
                act.wait_ge(s["qkn"], b + 1)
                A(PT[:, 0, :], QK, ACT.Copy).then_inc(s["p0"], 1)
                act.wait_ge(s["r1"], b + 1)
                A(PT[:, 1, :], QK, ACT.Copy).then_inc(s["p1"], 1)
                with act.Fori(0, PAIRS) as pr:
                    P = b * PAIRS + pr
                    for tl in range(0, 2 * NT, 2):
                        hh, i = divmod(tl, NT)
                        act.wait_ge(s["S"], P * 2 * NT + tl + 1)
                        A(arena[:, tl, :], bank2(tl % 4), ACT.Copy, scale=0.25, accum_out=SUM[:, hh, i:i + 1])\
                            .then_inc(s["eva"], 1)
                    for k in range(COUNTS):
                        for hh in range(2):
                            act.wait_ge(s["t"], P * 2 * COUNTS + 2 * k + hh + 1)
                            for i in range(NA):
                                m = (2 * k + hh) * NA + i
                                if m >= 4:
                                    act.wait_ge(s["ca"], P * 2 * COUNTS * NA + m - 3)
                                A(JAb[:, m % 4, :], arena[:, hh * NT + i, :], ACT.Sign, scale=-1.0, bias=TE[:, hh, 0, i:i + 1],
                                  accum_out=CA[:, hh, i:i + 1]).then_inc(s["ca"], 1)
                    for hh in range(2):
                        act.wait_ge(s["tt"], P * 2 + hh + 1)
                        A(TPT[:, hh, :], PS[0:24, 7, 0:128], ACT.Copy).then_inc(s["tpt"], 1)
                        for mt in range(NT):
                            n = hh * NT + mt
                            act.wait_ge(s["st"], P * 2 * NT + n + 1)
                            if n >= 2:
                                act.wait_ge(s["p"], P * 2 * NT + n - 1)
                            A(JA[:, mt % 2, :], bank2(mt % 2), ACT.Exp, scale=0.25).then_inc(s["e"], 1)
                    act.wait_ge(s["e"], P * 2 * NT + 2 * NT)
                    act.sem_inc(s["apair"], 1)
                act.wait_ge(s["ot"], b + 1)
                A(OC, bank2(0), ACT.Copy).then_inc(s["oc"], 1)
                act.wait_ge(s["cst"], b * 5 + 2)
                for k in range(3):
                    A(Y[:, k, :], bank2(k), ACT.Silu, scale=SC[:, k:k + 1], bias=SH[:, k:k + 1]).then_inc(s["y"], 1)
                act.wait_ge(s["cst"], b * 5 + 3)
                for k in range(3):
                    A(DL[:, 1 + k, :], bank2(k), ACT.Identity, scale=SC[:, k:k + 1], bias=SH[:, k:k + 1]).then_inc(s["dl"], 1)
                for k in range(16):
                    o, ch = divmod(k, 8)
                    act.wait_ge(s["f1"], b * 16 + k + 1)
                    A(HF[:, o, 512 * ch:512 * ch + 512], PS[:, k % 6, :], ACT.Copy).then_inc(s["hc"], 1)
                act.wait_ge(s["cst"], b * 5 + 4)
                for q in range(4):
                    for o in range(2):
                        v = HF[:, o, N0 * q:N0 * q + N0]
                        A(v, v, ACT.Gelu, scale=SC[:, o:o + 1], bias=SH[:, o:o + 1]).then_inc(s["ge"], 1)
                for ch in range(8):
                    act.wait_ge(s["f2"], b * 8 + ch + 1)
                    A(F2[:, 512 * ch:512 * ch + 512], PS[:, ch % 6, :], ACT.Copy).then_inc(s["f2c"], 1)
                act.wait_ge(s["cst"], b * 5 + 5)
                for q in range(4):
                    v = F2[:, N0 * q:N0 * q + N0]
                    A(v, v, ACT.Identity, scale=SC[:, 0:1], bias=SH[:, 0:1]).then_inc(s["f2n"], 1)
                act.wait_ge(s["q1"], b + 1)
                A(Q1, bank2(0), ACT.Identity, bias=vecs[:, V_BQK:V_BQK + 1]).then_inc(s["q1c"], 1)
                act.wait_ge(s["q1c"], b + 1)
                A(PT1[:, 0, :], Q1, ACT.Copy).then_inc(s["p10"], 1)
                for k in range(8):
                    act.wait_ge(s["v1p"], b * 8 + k + 1)
                    A(V1[:, 4 * k:4 * k + 4, 0:128], PS[:, 2 + k % 4, :].rearrange("p (m c) -> p m c", c=128), ACT.Copy)\
                        .then_inc(s["v1c"], 1)
                    if k == 3:
                        act.wait_ge(s["r11"], b + 1)
                        A(PT1[:, 1, :], Q1, ACT.Copy).then_inc(s["p11"], 1)

                def maxrow(k):
                    act.wait_ge(s["mt"], k)
                    A(MPT[:, :], PS[0:12, 3, 0:128], ACT.Copy).then_inc(s["mpt"], 1)

                def chunk(j, more):
                    J = b * NCH + j
                    for mt in range(MT1):
                        act.wait_ge(s["st1"], J * MT1 + mt + 1)
                        act.wait_ge(s["pv1"], J * MT1 + mt + 1)
                        A(P1[:, mt % 4, :], PS[:, 4 + mt % 2, :], ACT.Exp, scale=0.25).then_inc(s["e1"], 1)
                        if more and mt == 28:
                            maxrow(J + 2)

                maxrow(b * NCH + 1)
                with act.Fori(0, NCH - 1) as j:
                    chunk(j, True)
                chunk(NCH - 1, False)
                act.wait_ge(s["e1"], (b + 1) * NCH * MT1)
                act.sem_inc(s["enda"], 1)

        @block.vector
        def _(dve):
            V = nc.vector

            def stats_to_channels(ch, g, b, n):
                ch.wait()
                ch.link(V.tensor_tensor(ST[:, 0:n, 1], MV[:, 0:n, 0], MV[:, 0:n, 0], ALU.mult))
                ch.link(V.tensor_tensor(ST[:, 0:n, 1], ST[:, 0:n, 1], MV[:, 0:n, 1], ALU.add))
                V.tensor_copy(ST[:, 0:n, 0], MV[:, 0:n, 0]).then_inc(s["g1"], 1)
                dve.wait_ge(s["g2"], b * 5 + g + 1)
                ch.link(V.tensor_scalar(GG[:, :], PS[0:32, 7, 0:2], 1.0 / GN_CH[g], None, ALU.mult))
                ch.link(V.tensor_tensor(GV[:, 0:1], GG[:, 0:1], GG[:, 0:1], ALU.mult))
                ch.link(V.tensor_tensor(GV[:, 0:1], GG[:, 1:2], GV[:, 0:1], ALU.subtract))
                V.tensor_scalar(GV[:, 0:1], GV[:, 0:1], 0.0, 1e-6, ALU.max, ALU.add).then_inc(s["g3"], 1)
                dve.wait_ge(s["g5"], b * 5 + g + 1)
                bc = PS[:, 7, 8:8 + 2 * n].rearrange("p (k t) -> p k t", t=2)
                ch.link(V.tensor_tensor(SC[:, 0:n], bc[:, :, 1], vecs[:, GN_G[g]:GN_G[g] + n], ALU.mult))
                ch.link(V.tensor_tensor(SM[:, 0:n], bc[:, :, 0], SC[:, 0:n], ALU.mult))
                V.tensor_tensor(SH[:, 0:n], vecs[:, GN_B[g]:GN_B[g] + n], SM[:, 0:n],
                                ALU.subtract).then_inc(s["cst"], 1)
                dve.wait_ge(s["cst"], b * 5 + g + 1)

            ch = Chain(dve, s["dset"])
            ch.did(V.memset(VT[:, :, :, HD:HD + 1], 1.0))
            ch.did(V.memset(QPKP[KS:KA, 1], 1.0))
            ch.did(V.memset(PAD[:, :, :, :], 0.0))
            ch.did(V.memset(mhalf[:, :], -0.5))
            dve.sem_inc(s["xfree"], 1)
            dve.sem_inc(s["endd"], 1)
            dve.sem_inc(s["dpair"], 1)
            dve.sem_inc(s["on"], 1)
            dve.sem_inc(s["pv1"], 4)
            dve.sem_inc(s["out"], 16)
            dve.wait_ge(s["w"], 16 * 12)
            ch.did(V.tensor_copy(identb[:, :], ident))
            for t in range(27):
                ch.did(V.tensor_scalar(diag[:, t, :], ident, w_dw[:, t:t + 1], None, ALU.mult))
            for c, n in ((V_AG, 2), (V_F2G, 2), (V_H2G, 6)):
                ch.did(V.tensor_scalar(vecs[:, c:c + n], vecs[:, c:c + n], 0.1, None, ALU.mult))
            ch.wait()
            ch.did(V.tensor_scalar(vecs[:, V_H2G:V_H2G + 6], vecs[:, V_H2G:V_H2G + 6], vecs[:, V_ALPHA:V_ALPHA + 1], None, ALU.mult))
            dve.wait_ge(s["ws"], 1)
            ch.link(V.tensor_tensor(gbo[:, :], PS[:, 1, 0:1], vecs[:, V_BO:V_BO + 1], ALU.add))
            ch.link(V.tensor_tensor(gbo[:, :], gbo[:, :], vecs[:, V_GAMMA:V_GAMMA + 1], ALU.mult))
            assert ch.n == DSET, ch.n
            with dve.Fori(0, images) as b:
                ch = Chain(dve, s["dimg"])
                dve.wait_ge(s["ss"], b + 1)
                V.tensor_scalar(SSM[:, :], PS[:, 4, 0:128], 1e-24, None, ALU.max).then_inc(s["ssm"], 1)
                dve.wait_ge(s["rb"], b + 1)
                dve.wait_ge(s["qkc"], b + 1)
                V.tensor_tensor(QK, QK, PS[:, 4:8, :].rearrange("p a n -> p (a n)"), ALU.mult).then_inc(s["qkn"], 1)
                dve.wait_ge(s["p0"], b + 1)
                V.tensor_tensor(QK, QK, PT[:, 0, :], ALU.subtract).then_inc(s["r1"], 1)
                dve.wait_ge(s["p1"], b + 1)
                V.tensor_tensor(PT[:, 2, :], QK, PT[:, 1, :], ALU.subtract).then_inc(s["p2"], 1)
                with dve.Fori(0, PAIRS) as pr:
                    P = b * PAIRS + pr
                    cp = Chain(dve, s["dpr"])
                    for tl in range(1, 2 * NT, 2):
                        hh, i = divmod(tl, NT)
                        dve.wait_ge(s["S"], P * 2 * NT + tl + 1)
                        V.tensor_scalar(arena[:, tl, :], bank2(tl % 4), 0.25, None, ALU.mult, ALU.add,
                                        accum_out=SUM[:, hh, i:i + 1]).then_inc(s["evd"], 1)
                    dve.wait_ge(s["eva"], P * NT + NT)
                    dve.wait_ge(s["evd"], P * NT + NT)
                    cp.link(V.tensor_scalar(TE[:, :, 0, :], SUM[:, :, :], 1.0 / N0, None, ALU.mult))
                    cp.did(V.tensor_scalar(BR[:, :, 0, 0, :], TE[:, :, 0, :], -HALF, None, ALU.add))
                    cp.did(V.tensor_scalar(BR[:, :, 1, 0, :], TE[:, :, 0, :], HALF, None, ALU.add))
                    cp.did(V.memset(BR[:, :, 0, 1, :], HALF * SLOPE))
                    V.memset(BR[:, :, 1, 1, :], -HALF * SLOPE).then_inc(s["t"], 2)

                    def count(hh, k):
                        for i in range(NA, NT):
                            m = (2 * k + hh) * (NT - NA) + i - NA
                            if m >= 4:
                                dve.wait_ge(s["cd"], P * 2 * COUNTS * (NT - NA) + m - 3)
                            V.tensor_scalar(JDb[:, m % 4, :], arena[:, hh * NT + i, :], TE[:, hh, 0, i:i + 1], None,
                                            ALU.is_ge, ALU.add, accum_out=CD[:, hh, i:i + 1]).then_inc(s["cd"], 1)

                    def excess(hh, k):
                        dve.wait_ge(s["ca"], (P * 2 * COUNTS + 2 * k + hh + 1) * NA)
                        dve.wait_ge(s["cd"], (P * 2 * COUNTS + 2 * k + hh + 1) * (NT - NA))
                        cp.did(V.tensor_scalar(TE[:, hh, 1, 0:NA], CA[:, hh, 0:NA], -0.5, float(KEEP - AIM), ALU.mult, ALU.add))
                        cp.link(V.tensor_scalar(TE[:, hh, 1, NA:NT], CD[:, hh, NA:NT], float(-AIM), None, ALU.add))

                    def update(hh, k):
                        excess(hh, k)
                        e = TE[:, hh, 1, :]
                        cp.did(V.tensor_scalar(MK[:, hh, 0, :], e, 0.0, None, ALU.is_gt))
                        cp.did(V.tensor_scalar(MK[:, hh, 1, :], e, 0.0, None, ALU.is_le))
                        cp.did(V.tensor_tensor(E2[:, hh, :], e, e, ALU.mult))
                        cp.wait()
                        for end in range(2):
                            last = V.copy_predicated(BR[:, hh, end], MK[:, hh, end:end + 1, :].to_broadcast([128, 2, NT]), TE[:, hh])
                            cp.did(last)
                        cp.wait()
                        cp.link(V.tensor_tensor(DD[:, hh], BR[:, hh, 0], BR[:, hh, 1], ALU.subtract))
                        cp.did(V.tensor_scalar(MK2[:, hh, :], E2[:, hh, :], 3.25 ** 2, None, ALU.is_gt))
                        cp.link(V.reciprocal(DR[:, hh, :], DD[:, hh, 1, :]))
                        cp.link(V.tensor_tensor(DR[:, hh, :], DR[:, hh, :], BR[:, hh, 0, 1, :], ALU.mult))
                        cp.link(V.tensor_tensor(DR[:, hh, :], DR[:, hh, :], DD[:, hh, 0, :], ALU.mult))
                        cp.link(V.tensor_tensor(TN[:, hh, :], BR[:, hh, 0, 0, :], DR[:, hh, :], ALU.subtract))
                        V.copy_predicated(TE[:, hh, 0, :], MK2[:, hh, :], TN[:, hh, :]).then_inc(s["t"], 1)

                    for k in range(COUNTS):
                        for hh in range(2):
                            dve.wait_ge(s["t"], P * 2 * COUNTS + 2 * k + hh + 1)
                            count(hh, k)
                            if hh == 1 and k < COUNTS - 1:
                                update(0, k)
                            if hh == 0 and k >= 1:
                                update(1, k - 1)

                    def top8(hh, i):
                        z = JD[:, i % 2, :]
                        cp.link(V.scalar_tensor_tensor(z, arena[:, hh * NT + i, :], TE[:, hh, 0, i:i + 1],
                                                       arena[:, hh * NT + i, :], ALU.is_ge, ALU.subtract, reverse1=True))
                        cp.did(V.max(M8[:, hh, i, :], z))

                    def bisect(hh):
                        a, S4 = BR[:, hh], arena[:, hh * NT:hh * NT + NT]
                        V.memset(a[:, 0, 0, :], -0.2502)
                        V.memset(a[:, 1, 0, :], 0.2502)
                        dve.drain()
                        with dve.Fori(0, BISECT):
                            V.tensor_tensor(TN[:, hh, :], a[:, 0, 0, :], a[:, 1, 0, :], ALU.add)
                            dve.drain()
                            V.tensor_scalar(TN[:, hh, :], TN[:, hh, :], 0.5, None, ALU.mult)
                            dve.drain()
                            for i in range(NT):
                                V.tensor_scalar(JDb[:, i % 4, :], S4[:, i], TN[:, hh, i:i + 1], None, ALU.is_ge, ALU.add,
                                                accum_out=CD[:, hh, i:i + 1])
                                dve.drain()
                            V.tensor_scalar(MK[:, hh, 0, :], CD[:, hh, :], float(KEEP), None, ALU.is_ge)
                            V.tensor_scalar(MK[:, hh, 1, :], CD[:, hh, :], float(KEEP), None, ALU.is_lt)
                            dve.drain()
                            V.copy_predicated(a[:, 0, 0, :], MK[:, hh, 0, :], TN[:, hh, :])
                            V.copy_predicated(a[:, 1, 0, :], MK[:, hh, 1, :], TN[:, hh, :])
                            dve.drain()
                        for i in range(NT):
                            V.scalar_tensor_tensor(JD[:, i % 2, :], S4[:, i], a[:, 0, 0, i:i + 1], S4[:, i], ALU.is_ge,
                                                   ALU.subtract, reverse1=True)
                            dve.drain()
                            V.reduce_max(TN[:, hh, i:i + 1], JD[:, i % 2, :], AX.X)
                            dve.drain()
                        V.tensor_tensor(TS[:, hh, :], a[:, 0, 0, :], TN[:, hh, :], ALU.add)
                        dve.drain()

                    def threshold(hh):
                        cp.did(V.tensor_tensor(OH[:, hh], TE[:, hh, 1, :].unsqueeze(2).to_broadcast([128, NT, 7]),
                                               window.unsqueeze(1).to_broadcast([128, NT, 7]), ALU.subtract))
                        cp.wait()
                        cp.link(V.tensor_tensor(OH[:, hh], OH[:, hh], OH[:, hh], ALU.mult))
                        cp.did(V.tensor_scalar(OH[:, hh], OH[:, hh], 0.25, None, ALU.is_lt))
                        cp.link(V.tensor_tensor(PM[:, hh], M8[:, hh, :, 0:7], M8[:, hh, :, 1:8], ALU.add))
                        cp.link(V.tensor_tensor(PM[:, hh], PM[:, hh], OH[:, hh], ALU.mult))
                        cp.did(V.tensor_reduce(TS[:, hh, :], PM[:, hh], AX.X, ALU.add))
                        V.tensor_reduce(FOUND[:, hh, :], OH[:, hh], AX.XY, ALU.add).then_inc(s["fnd"], 1)
                        dve.wait_ge(s["fsum"], P * 2 + hh + 1)
                        cp.link(V.tensor_scalar(FOUNDI[:, :], PS[0:1, 7, 256:257], -2.0, None, ALU.mult))
                        found = dve.value_load(FOUNDI[0:1, 0:1], min_val=0, max_val=N0)
                        with dve.If(found < N0):
                            bisect(hh)
                        cp.link(V.tensor_scalar(TP[:, hh, 0, :], TS[:, hh, :], -2.0, None, ALU.mult))
                        cp.link(V.scalar_tensor_tensor(TR[:, hh, :], TS[:, hh, :], -2.0, TP[:, hh, 0, :], ALU.mult, ALU.subtract))
                        cp.link(V.tensor_copy(TP[:, hh, 1, :], TR[:, hh, :]))
                        V.tensor_tensor(TP[:, hh, 2, :], TR[:, hh, :], TP[:, hh, 1, :], ALU.subtract).then_inc(s["tp"], 1)

                    def mask(hh, mt):
                        n = hh * NT + mt
                        dve.wait_ge(s["e"], P * 2 * NT + n + 1)
                        V.scalar_tensor_tensor(arena[:, n, :], bank2(mt % 2), 0.0, JA[:, mt % 2, :], ALU.is_ge, ALU.mult)\
                            .then_inc(s["p"], 1)

                    def heads_out(hh):
                        dve.wait_ge(s["pv"], P * 2 + hh + 1)
                        sums = PS[:, 6, 0:17 * NT].rearrange("p (i d) -> p i d", d=17)
                        cp.link(V.reciprocal(RO[:, :], sums[:, :, 16]))
                        V.tensor_tensor(O[:, :, bass.ds(pr * 2 + hh, 1), :].rearrange("p i h d -> p i (h d)"), sums[:, :, 0:16],
                                        RO[:, :].unsqueeze(2).to_broadcast([128, NT, 16]), ALU.mult).then_inc(s["o"], 1)

                    excess(0, COUNTS - 1)
                    for i in range(NT):
                        top8(0, i)
                    threshold(0)
                    excess(1, COUNTS - 1)
                    for i in range(NT):
                        top8(1, i)
                        mask(0, i)
                    threshold(1)
                    mask(1, 0)
                    heads_out(0)
                    for mt in range(1, NT):
                        mask(1, mt)
                    heads_out(1)
                    dve.wait_ge(s["o"], P * 2 + 2)
                    dve.sem_inc(s["dpair"], 1)
                    cp.wait()
                dve.wait_ge(s["pj"], b + 1)
                for h in range(2):
                    ch.did(V.bn_stats(BN[:, h, :], PS[:, 2 + h, :]))
                ch.wait()
                ch.did(V.bn_aggr(MV[:, 0, :], BN[:, 0:2, :].rearrange("p a s -> p (a s)")))
                stats_to_channels(ch, 0, b, 1)
                V.tensor_scalar(DL[:, 0, :], bank2(1), SC[:, 0:1], SH[:, 0:1], ALU.mult, ALU.add).then_inc(s["dll"], 1)
                dve.wait_ge(s["dll"], b + 1)
                for g, src in ((1, "cv"), (2, "pw")):
                    for k in range(3):
                        dve.wait_ge(s[src], b * 3 + k + 1)
                        for h in range(2):
                            ch.did(V.bn_stats(BN[:, 2 * k + h, :], PS[:, 2 * k + h, :]))
                    ch.wait()
                    for k in range(3):
                        ch.did(V.bn_aggr(MV[:, k, :], BN[:, 2 * k:2 * k + 2, :].rearrange("p a s -> p (a s)")))
                    stats_to_channels(ch, g, b, 3)
                xi = Xin[:, :].rearrange("p (y a x c) -> p y a x c", a=2, x=HH, c=2)
                xo = X1[:, :].rearrange("p (y a x c) -> p y a x c", a=2, x=HH, c=2)
                for k, (a, c) in enumerate(((0, 0), (1, 0), (0, 1), (1, 1))):
                    dve.wait_ge(s["iw"], b * 4 + k + 1)
                    last = V.scalar_tensor_tensor(xo[:, :, a, :, c], xi[:, :, a, :, c], 1.2,
                                                  IX[:, k, :].rearrange("p (y x) -> p y x", x=HH), ALU.mult, ALU.add)
                    last.then_inc(s["x1"], 1)
                dve.wait_ge(s["x1"], (b + 1) * 4)
                dve.sem_inc(s["xfree"], 1)
                for k in range(16):
                    o, c8 = divmod(k, 8)
                    dve.wait_ge(s["hc"], b * 16 + k + 1)
                    ch.did(V.bn_stats(BN[:, k, :], HF[:, o, 512 * c8:512 * c8 + 512]))
                ch.wait()
                for o in range(2):
                    ch.did(V.bn_aggr(MV[:, o, :], BN[:, 8 * o:8 * o + 8, :].rearrange("p a s -> p (a s)")))
                stats_to_channels(ch, 3, b, 2)
                for k in range(8):
                    dve.wait_ge(s["f2c"], b * 8 + k + 1)
                    ch.did(V.bn_stats(BN[:, k, :], F2[:, 512 * k:512 * k + 512]))
                ch.wait()
                ch.did(V.bn_aggr(MV[:, 0, :], BN[:, 0:8, :].rearrange("p a s -> p (a s)")))
                stats_to_channels(ch, 4, b, 1)
                for q in range(4):
                    dve.wait_ge(s["f2n"], b * 4 + q + 1)
                    v = X1[:, N0 * q:N0 * q + N0]
                    V.tensor_tensor(v, v, F2[:, N0 * q:N0 * q + N0], ALU.add).then_inc(s["x2"], 1)
                ch.did(V.memset(V1[:, :, 128:129], 1.0))
                dve.wait_ge(s["p10"], b + 1)
                V.tensor_tensor(Q1, Q1, PT1[:, 0, :], ALU.subtract).then_inc(s["r11"], 1)
                dve.wait_ge(s["p11"], b + 1)
                V.tensor_tensor(PT1[:, 2, :], Q1, PT1[:, 1, :], ALU.subtract).then_inc(s["p12"], 1)
                ch.wait()

                def maxima(k, base):
                    i, c8 = divmod(k, NCH)
                    dve.wait_ge(s["m"], base + k + 1)
                    V.reduce_max(MX[:, i, c8:c8 + 1], PS[:, k % 3, :], AX.X).then_inc(s["mr"], 1)

                def parts(cc, base):
                    dve.wait_ge(s["mr"], base + 32)
                    cc.link(V.tensor_reduce(MM[:, :], MX[:, :, :], AX.X, ALU.max))
                    cc.link(V.tensor_scalar(MP[:, 0, :], MM[:, :], -1.0, None, ALU.mult))
                    cc.link(V.scalar_tensor_tensor(MR[:, :], MM[:, :], -1.0, MP[:, 0, :], ALU.mult, ALU.subtract))
                    cc.link(V.tensor_copy(MP[:, 1, :], MR[:, :]))
                    V.tensor_tensor(MP[:, 2, :], MR[:, :], MP[:, 1, :], ALU.subtract).then_inc(s["mp"], 1)

                def chunk(j, more):
                    J = b * NCH + j
                    cc = Chain(dve, s["dch"])
                    if more:
                        for k in range(32):
                            maxima(k, (J + 1) * 32)
                        parts(cc, (J + 1) * 32)
                    dve.wait_ge(s["pv1"], (J + 1) * MT1 + 4)
                    sums = PS[:, 6:8, 0:272].rearrange("p k (i c) -> p k i c", c=136)
                    rd = RD[:, :].rearrange("p (k i) -> p k i", i=2)
                    cc.link(V.reciprocal(rd, sums[:, :, :, 128]))
                    cc.link(V.tensor_scalar(RD[:, :], RD[:, :], vecs[:, V_GAMMA:V_GAMMA + 1], None, ALU.mult))
                    for i in range(4):
                        last = V.tensor_scalar(ON[:, i, :], sums[:, i // 2, i % 2, 0:128], RD[:, i:i + 1], None, ALU.mult)
                    last.then_inc(s["on"], 1)
                    dve.wait_ge(s["nt"], J + 1)
                    dve.wait_ge(s["out"], (J + 1) * 16)
                    V.scalar_tensor_tensor(YO[:, 0, :], PS[:, 3, :], gbo[:, 0:1], X1[:, bass.ds(j * 512, 512)],
                                           ALU.add, ALU.add).then_inc(s["y1"], 1)

                c0 = Chain(dve, s["dch"])
                for k in range(32):
                    maxima(k, b * NCH * 32)
                parts(c0, b * NCH * 32)
                with dve.Fori(0, NCH - 1) as j:
                    chunk(j, True)
                chunk(NCH - 1, False)
                dve.wait_ge(s["y1"], (b + 1) * NCH)
                dve.sem_inc(s["endd"], 1)

        @block.gpsimd
        def _(pool):
            G = nc.gpsimd
            TT = G.tensor_tensor
            pool.wait_ge(s["dset"], DSET)

            def power(b, g):
                pool.wait_ge(s["g3"], b * 5 + g + 1)
                TT(GG[:, 1:2], GV[:, 0:1], mhalf[0:32, 0:1], ALU.pow).then_inc(s["g4"], 1)

            with pool.Fori(0, images) as b:
                pool.sem_clear(s["pimg"])
                pool.wait_ge(s["xin"], (b + 1) * 16)
                pool.wait_ge(s["endd"], b + 1)
                pool.wait_ge(s["enda"], b + 1)
                v = Xin[:, :].rearrange("p (y a x c) -> p y a x c", a=2, x=HH, c=2)
                x1, x2, x3, x4 = v[:, :, 0, :, 0], v[:, :, 1, :, 0], v[:, :, 0, :, 1], v[:, :, 1, :, 1]
                d = [DW[:, k, :].rearrange("p (y x) -> p y x", x=HH) for k in range(4)]
                TT(d[0], x1, x2, ALU.add).then_inc(s["pimg"], 1)
                TT(d[1], x3, x4, ALU.add).then_inc(s["pimg"], 1)
                TT(d[2], x2, x1, ALU.subtract).then_inc(s["pimg"], 1)
                TT(d[3], x4, x3, ALU.subtract).then_inc(s["pimg"], 1)
                pool.wait_ge(s["pimg"], 4)
                for k, (p, q, op) in enumerate(((0, 1, ALU.add), (1, 0, ALU.subtract), (2, 3, ALU.add), (3, 2, ALU.subtract))):
                    TT(UU[:, k, :], DW[:, p, :], DW[:, q, :], op).then_inc(s["dwt"], 1)
                pool.wait_ge(s["dwt"], (b + 1) * 4)
                pool.wait_ge(s["ssm"], b + 1)
                TT(RN[:, :], SSM[:, :], mhalf[:, :], ALU.pow).then_inc(s["pimg"], 1)
                pool.wait_ge(s["pimg"], 5)
                G.tensor_copy(RE.rearrange("p k (h d) -> p (k h) d", d=HD),
                              RN[:, :].unsqueeze(2).to_broadcast([128, 128, HD])).then_inc(s["re"], 1)
                power(b, 0)
                power(b, 1)
                power(b, 2)
                pool.wait_ge(s["dll"], b + 1)
                pool.wait_ge(s["dl"], (b + 1) * 3)
                for k, (p, q, op) in enumerate(((0, 1, ALU.subtract), (0, 1, ALU.add), (2, 3, ALU.subtract), (2, 3, ALU.add))):
                    TT(IW[:, k, :], DL[:, p, :], DL[:, q, :], op).then_inc(s["pimg"], 1)
                pool.wait_ge(s["pimg"], 9)
                for k, (p, q, op) in enumerate(((0, 2, ALU.subtract), (0, 2, ALU.add), (1, 3, ALU.subtract), (1, 3, ALU.add))):
                    TT(IX[:, k, :], IW[:, p, :], IW[:, q, :], op).then_inc(s["iw"], 1)
                power(b, 3)
                power(b, 4)


DSET = 38


_SHAPE = (B, C, H, W)


def laid_out(inputs):
    f = {k: np.asarray(v) for k, v in inputs.items()}
    L0 = {k[8:]: v for k, v in f.items() if k.startswith("L0_conv_")}
    L1 = {k[8:]: v for k, v in f.items() if k.startswith("L1_conv_")}
    c = np.ascontiguousarray

    def cols(v):
        return v.reshape(-1, 128).T

    bqk = np.tile(np.concatenate([L1["bq"], L1["bk"]]), 4).reshape(128, 1)
    vec = np.concatenate([
        cols(L0["attn_gn_g"]), cols(L0["attn_gn_b"]), cols(L0["he_gn1_g"]), cols(L0["he_gn1_b"]),
        cols(L0["he_gn2_g"]), cols(L0["he_gn2_b"]), cols(L0["ffn_gn1_g"]), cols(L0["ffn_gn1_b"]),
        cols(L0["ffn_gn2_g"]), cols(L0["ffn_gn2_b"]), bqk, cols(L1["bv"]), cols(L1["bo"]),
        np.broadcast_to(L0["alpha"].reshape(1, 1), (128, 1)), np.broadcast_to(L1["gamma"].reshape(1, 1), (128, 1))], axis=1)
    p = np.arange(128)
    ind = np.zeros((128, 6, 32), np.float32)
    for k, (blk, per) in enumerate(((0, 4), (0, 12), (1, 12), (2, 12), (0, 8), (1, 8))):
        ind[p, k, (blk * 128 + p) // per] = 1
    head = np.zeros((128, 8), np.float32)
    head[p, p // HD] = 1
    win = np.broadcast_to(3 - np.arange(7, dtype=np.float32) - 0.25, (128, 7))
    cst = np.concatenate([np.eye(128, dtype=np.float32), head, win, ind.reshape(128, -1)], axis=1)
    return {
        "x": c(f["x"].reshape(B, C, N1)), "qkvT": c(L0["qkv_w"].T), "projT": c(L0["proj_w"].T),
        "dw": c(L0["he_dw_w"].reshape(3, 128, 9).transpose(1, 0, 2).reshape(128, 27)),
        "pwT": c(L0["he_pw_w"].T.reshape(3, 128, 384).transpose(1, 0, 2)), "w1T": c(L0["ffn_w1"].T),
        "w2T": c(L0["ffn_w2"].T.reshape(2, 128, 128).transpose(1, 0, 2)),
        "qk1T": c(np.concatenate([L1["Wq"], L1["Wk"]]).T), "wv": c(L1["Wv"]), "woT": c(L1["Wo"].T),
        "vec": c(vec), "cst": c(cst), "cstT": c(ind.transpose(2, 1, 0)),
    }


def kernel(**inputs):
    import concourse.bacc as _bacc
    from concourse.bass_utils import run_bass_kernel_spmd as _run

    nc = _bacc.Bacc("TRN2", target_bir_lowering=False, num_devices=1)
    arrays = laid_out(inputs)
    args = [nc.dram_tensor(f"in_{k}", a.shape, mybir.dt.float32, kind="ExternalInput").ap() for k, a in arrays.items()]
    out = nc.dram_tensor("out_0", (B, C, N1), mybir.dt.float32, kind="ExternalOutput").ap()
    dwt_attention_kernel(nc, *args, out)
    r = _run(nc, [{f"in_{k}": a for k, a in arrays.items()}], core_ids=[0])
    return r.results[0]["out_0"].reshape(_SHAPE)
```
